# Optimizing a Trainium2 kernel written in Bass

```python
import numpy as np
import jax
import jax.numpy as jnp

def _softmax(x, axis=-1):
    return jax.nn.softmax(x, axis=axis)

def _gelu(x):
    return jax.nn.gelu(x, approximate=True)

def _silu(x):
    return jax.nn.silu(x)

def _sigmoid(x):
    return jax.nn.sigmoid(x)

def _layernorm(x, axis=-1, eps=1e-05):
    m = jnp.mean(x, axis=axis, keepdims=True)
    v = jnp.var(x, axis=axis, keepdims=True)
    return (x - m) / jnp.sqrt(v + eps)

def _scatter_add(tgt, idx, src, axis=0):
    return tgt.at[idx].add(src)

def _segment_sum(src, seg, n):
    return jax.ops.segment_sum(src, seg, n)
kernel_name = 'mk_cond_seq_d1_seqx_r4_ce6ba9'

def setup_inputs(seed: int=0):
    np.random.seed(seed)
    _w = jnp.asarray

    def _rec_inputs():
        import jax
        import jax.numpy as jnp
        _rk = jax.random.key(seed)
        x = -0.000125 + 0.9999 * jax.random.normal(jax.random.fold_in(_rk, 1), (8, 256, 256), jnp.float32)
        _lenS = 256 - jax.random.randint(jax.random.fold_in(_rk, 7), (8,), 0, max(1, 256 // 4) + 1, jnp.int32)
        _lenS2 = 256 - jax.random.randint(jax.random.fold_in(_rk, 8), (8,), 0, max(1, 256 // 4) + 1, jnp.int32)
        cond_1024 = 0.000887014 + 1.03683 * jax.random.normal(jax.random.fold_in(_rk, 11), (8, 256), jnp.float32)
        return (x, cond_1024)
    x, cond_1024 = _rec_inputs()

    def _L0_cond_setup():
        import jax, jax.numpy as jnp
        import numpy as np
        EPS = 1e-06
        WINDOW = 256
        NUM_HEADS = 16

        def _layernorm(x):
            mu = jnp.mean(x, axis=-1, keepdims=True)
            var = jnp.mean(jnp.square(x - mu), axis=-1, keepdims=True)
            return (x - mu) * jax.lax.rsqrt(var + EPS)

        def _windowed_attn(h, w_qkv, b_qkv, w_proj, b_proj):
            B, T, C = h.shape
            H = NUM_HEADS
            d = C // H
            Nw = T // WINDOW
            qkv = h @ w_qkv + b_qkv
            qkv = qkv.reshape(B, Nw, WINDOW, 3, H, d)
            q, k, v = (qkv[..., 0, :, :], qkv[..., 1, :, :], qkv[..., 2, :, :])
            scores = jnp.einsum('bnihd,bnjhd->bnhij', q, k) * d ** (-0.5)
            attn = jax.nn.softmax(scores, axis=-1)
            out = jnp.einsum('bnhij,bnjhd->bnihd', attn, v).reshape(B, T, C)
            return out @ w_proj + b_proj
        key = jax.random.key(seed)
        ks = jax.random.split(key, 16)
        B, T, C = (2, 4096, 256)
        Dff = 4 * C
        s = lambda fan_in: 1.0 / np.sqrt(fan_in)
        inp = {'x': jax.random.normal(ks[0], (B, T, C), jnp.float32), 'c': jax.random.normal(ks[1], (B, C), jnp.float32), 'w_qkv': jax.random.normal(ks[2], (C, 3 * C), jnp.float32) * s(C), 'b_qkv': jnp.zeros((3 * C,), jnp.float32), 'w_proj': jax.random.normal(ks[3], (C, C), jnp.float32) * s(C), 'b_proj': jnp.zeros((C,), jnp.float32), 'w_ada': jax.random.normal(ks[4], (C, 6 * C), jnp.float32) * s(C), 'b_ada': jnp.zeros((6 * C,), jnp.float32), 'w1': jax.random.normal(ks[5], (C, Dff), jnp.float32) * s(C), 'b1': jnp.zeros((Dff,), jnp.float32), 'w2': jax.random.normal(ks[6], (Dff, C), jnp.float32) * s(Dff), 'b2': jnp.zeros((C,), jnp.float32)}
        return inp
    _L0_cond_all = _L0_cond_setup()
    _L0_cond_in = {k: v for k, v in _L0_cond_all.items() if k in ('w_qkv', 'b_qkv', 'w_proj', 'b_proj', 'w_ada', 'b_ada', 'w1', 'b1', 'w2', 'b2')}
    del _L0_cond_all
    return {'x': x, 'cond_1024': cond_1024, 'L0_cond_w_qkv': _L0_cond_in['w_qkv'], 'L0_cond_b_qkv': _L0_cond_in['b_qkv'], 'L0_cond_w_proj': _L0_cond_in['w_proj'], 'L0_cond_b_proj': _L0_cond_in['b_proj'], 'L0_cond_w_ada': _L0_cond_in['w_ada'], 'L0_cond_b_ada': _L0_cond_in['b_ada'], 'L0_cond_w1': _L0_cond_in['w1'], 'L0_cond_b1': _L0_cond_in['b1'], 'L0_cond_w2': _L0_cond_in['w2'], 'L0_cond_b2': _L0_cond_in['b2']}

def reference(x, cond_1024, L0_cond_w_qkv, L0_cond_b_qkv, L0_cond_w_proj, L0_cond_b_proj, L0_cond_w_ada, L0_cond_b_ada, L0_cond_w1, L0_cond_b1, L0_cond_w2, L0_cond_b2):
    import jax
    import jax.numpy as jnp

    def _L0_cond_ref(x, c, w_qkv, b_qkv, w_proj, b_proj, w_ada, b_ada, w1, b1, w2, b2):
        import jax, jax.numpy as jnp
        import numpy as np
        EPS = 1e-06
        WINDOW = 256
        NUM_HEADS = 16

        def _layernorm(x):
            mu = jnp.mean(x, axis=-1, keepdims=True)
            var = jnp.mean(jnp.square(x - mu), axis=-1, keepdims=True)
            return (x - mu) * jax.lax.rsqrt(var + EPS)

        def _windowed_attn(h, w_qkv, b_qkv, w_proj, b_proj):
            B, T, C = h.shape
            H = NUM_HEADS
            d = C // H
            Nw = T // WINDOW
            qkv = h @ w_qkv + b_qkv
            qkv = qkv.reshape(B, Nw, WINDOW, 3, H, d)
            q, k, v = (qkv[..., 0, :, :], qkv[..., 1, :, :], qkv[..., 2, :, :])
            scores = jnp.einsum('bnihd,bnjhd->bnhij', q, k) * d ** (-0.5)
            attn = jax.nn.softmax(scores, axis=-1)
            out = jnp.einsum('bnhij,bnjhd->bnihd', attn, v).reshape(B, T, C)
            return out @ w_proj + b_proj
        mod = jax.nn.silu(c) @ w_ada + b_ada
        C = x.shape[-1]
        shift_msa, scale_msa, gate_msa, shift_mlp, scale_mlp, gate_mlp = [mod[:, i * C:(i + 1) * C][:, None, :] for i in range(6)]
        h = _layernorm(x)
        h = h * (1.0 + scale_msa) + shift_msa
        h = _windowed_attn(h, w_qkv, b_qkv, w_proj, b_proj)
        x = x + h * gate_msa
        h = _layernorm(x)
        h = h * (1.0 + scale_mlp) + shift_mlp
        h = jax.nn.gelu(h @ w1 + b1, approximate=True) @ w2 + b2
        x = x + h * gate_mlp
        return x
    x = _L0_cond_ref(x, cond_1024, L0_cond_w_qkv, L0_cond_b_qkv, L0_cond_w_proj, L0_cond_b_proj, L0_cond_w_ada, L0_cond_b_ada, L0_cond_w1, L0_cond_b1, L0_cond_w2, L0_cond_b2)
    return x

_drawn_inputs = setup_inputs


def setup_inputs(seed=0):
    import zlib

    import numpy as np

    out = dict(_drawn_inputs(seed))
    spreads = {'L0_cond_b_qkv': (0.0, 0.1),
     'L0_cond_b_proj': (0.0, 0.1),
     'L0_cond_b_ada': (0.0, 0.1),
     'L0_cond_b1': (0.0, 0.1),
     'L0_cond_b2': (0.0, 0.1)}
    factors = {}
    for name, (base, spread) in spreads.items():
        noise = np.random.default_rng([zlib.crc32(name.encode()), seed]).standard_normal(out[name].shape)
        drawn = base * np.exp(spread * noise) if base else spread * noise
        out[name] = jnp.asarray(drawn.astype(out[name].dtype))
    for name, factor in factors.items():
        out[name] = (out[name] * factor).astype(out[name].dtype)
    return out
```

```python
import concourse.bass as bass
from concourse import mybir
from contextlib import ExitStack


F32 = mybir.dt.float32
F32R = mybir.dt.float32r
ALU = mybir.AluOpType
ACT = mybir.ActivationFunctionType
AX = mybir.AxisListType

P = 128
EPS = 1e-6
ZROW = 48

TENSOR_STEPS = ["cond_T", "bias_T", "mod_T", "qkv_bias", "gate_rows", "proj_bias", "mlp_bias"]
SCALAR_STEPS = ["exp_cond", "wqkv_hi", "wp_hi", "w1_hi", "w2_hi"]
VECTOR_STEPS = ["plus_one", "recip", "silu", "bias_T", "mod_msa", "mod_mlp", "scale_msa", "scale_mlp",
                "wqkv_lo", "qkv_bias", "gate_rows", "proj_bias", "gate_proj_bias", "gate_mlp_bias",
                "wp_lo", "mlp_bias"]
POOL_STEPS = ["minus_half", "eps", "ident_zero", "ident", "zero_rows", "v_zero0", "v_zero1", "v_one0", "v_one1", "q_stack0", "k_stack0",
              "q_stack1", "k_stack1", "w1_lo", "w2_lo"]


def done(steps, name):
    return steps.index(name) + 1


def adaln_block_kernel(nc, x, cond, w_qkv, b_qkv, w_proj, b_proj, w_ada, b_ada, w1, b1, w2, b2, out):
    B, T, C = x.shape
    F = w1.shape[1]
    H = 16
    D = C // H
    SCALE = float(D) ** -0.5
    KC = C // P
    NT = T // P
    FT = F // P
    HG = 4
    NCH = (H // HG) * NT
    NMX = (H // 2) * NT
    NF1 = FT // 2
    assert D == 16 and KC == 2 and NT == 2 and B % 2 == 0 and B >= 6

    R_ADA, R_QKV, R_B1 = 0, 6 * KC, 9 * KC
    NROW = R_B1 + FT
    SHIFT1, SCALE1, SHIFT2, SCALE2 = 0, KC, 3 * KC, 4 * KC

    qk_scr = nc.dram_tensor("qk_scratch", [4, C, T], F32, kind="Internal").ap()
    gate_scr = nc.dram_tensor("gate_scratch", [B, 4 * C], F32, kind="Internal").ap()

    max_scr = nc.dram_tensor("max_scratch", [2, 2, H, T], F32, kind="Internal").ap()

    ctx = ExitStack()
    with ctx:
        def sb(name, shape, dt=F32):
            return ctx.enter_context(nc.sbuf_tensor(name, shape, dt))

        def sem(name):
            return ctx.enter_context(nc.semaphore(name))

        wqkv_hi = sb("wqkv_hi", [P, KC, 3 * C], F32R)
        wqkv_lo = sb("wqkv_lo", [P, KC, 3 * C], F32R)
        wp_hi = sb("wp_hi", [P, KC, C], F32R)
        wp_lo = sb("wp_lo", [P, KC, C], F32R)
        w1_hi = sb("w1_hi", [P, KC, F], F32R)
        w1_lo = sb("w1_lo", [P, KC, F], F32R)
        w2_hi = sb("w2_hi", [P, FT, C], F32R)
        w2_lo = sb("w2_lo", [P, FT, C], F32R)
        q_stack = [sb(f"q_stack{i}", [P, H, T], F32R) for i in range(2)]
        k_stack = [sb(f"k_stack{i}", [P, H, T], F32R) for i in range(2)]
        v_ext = [sb(f"v_ext{i}", [P, NT, H, 32]) for i in range(2)]
        probs = sb("probs", [P, 4, HG * T])
        gelu = sb("gelu", [P, FT, T])
        g_hi = sb("g_hi", [P, FT, T], F32R)
        g_lo = sb("g_lo", [P, FT, T], F32R)
        x_in = sb("x_in", [P, NT, C])
        x_res = sb("x_res", [P, NT, C])
        x2 = sb("x2", [P, NT, C])
        result = sb("result", [P, NT, C])
        x2g = sb("x2g", [P, NT, C])
        xn = sb("xn", [P, NT, C])
        h1_hi = sb("h1_hi", [P, KC, T], F32R)
        h1_lo = sb("h1_lo", [P, KC, T], F32R)
        h2_hi = sb("h2_hi", [P, KC, T], F32R)
        h2_lo = sb("h2_lo", [P, KC, T], F32R)
        qk_hi = sb("qk_hi", [P, 2 * KC, T], F32R)
        qk_lo = sb("qk_lo", [P, 2 * KC, T], F32R)
        o_raw = sb("o_raw", [P, H // HG, T])
        o_tok = sb("o_tok", [P, NT, C])
        oT_hi = sb("oT_hi", [P, KC, T], F32R)
        oT_lo = sb("oT_lo", [P, KC, T], F32R)
        gates = sb("gates", [P, 4, C])
        neg_max = sb("neg_max", [P, NT, H])
        m_hi = sb("m_hi", [H, T], F32R)
        m_lo = sb("m_lo", [H, T], F32R)
        den_rec = sb("den_rec", [P, NT * H])
        stats1 = sb("stats1", [P, NT, 6])
        stats2 = sb("stats2", [P, NT, 6])
        mv1 = sb("mv1", [P, NT, 2])
        mv2 = sb("mv2", [P, NT, 2])
        ve1 = sb("ve1", [P, NT])
        ve2 = sb("ve2", [P, NT])
        rstd1 = sb("rstd1", [P, NT])
        rstd2 = sb("rstd2", [P, NT])
        eps = sb("eps", [P, NT])
        minus_half = sb("minus_half", [P, NT])
        ident = sb("ident", [P, P])
        zero_rows = sb("zero_rows", [H, T])
        bias_T = sb("bias_T", [P, NROW])
        cond_T = sb("cond_T", [P, KC, B])
        exp_c = sb("exp_c", [P, KC, B])
        silu_T = sb("silu_T", [P, KC, B])
        mod_T = sb("mod_T", [P, 6 * KC, B])
        qkv_bias = sb("qkv_bias", [P, 3 * KC, B])
        mlp_bias = sb("mlp_bias", [P, FT, B])

        probs_flat = probs[:, :, :].rearrange("p s n -> p (s n)")
        gelu_flat = gelu[:, :, :].rearrange("p f t -> p (f t)")
        wada_raw = probs_flat[:, 0:KC * 6 * C].rearrange("p (k n) -> p k n", k=KC)
        wp_raw = probs_flat[:, KC * 6 * C:KC * 7 * C].rearrange("p (k n) -> p k n", k=KC)
        w1_raw = probs_flat[:, 0:KC * F].rearrange("p (k n) -> p k n", k=KC)
        wqkv_raw = gelu_flat[:, 0:KC * 3 * C].rearrange("p (k n) -> p k n", k=KC)
        w2_raw = gelu_flat[:, 0:FT * C].rearrange("p (k n) -> p k n", k=FT)
        cond_sb = xn[0:B, 0, :]
        bias_rows = xn[0:NROW, 1, 0:P]
        rows = o_raw[0:B, :, :]
        row_bias = gates[0:B, :, :]

        ps = ctx.enter_context(nc.psum_tensor("ps", [P, 8, 512], F32))

        def halves(bank):
            return ps[:, bank, :].rearrange("p (a n) -> p a n", a=2)

        s_cond, s_bias, s_wada, s_wqkv, s_wp, s_rowb, s_w1, s_w2 = (
            sem(n) for n in ("s_cond", "s_bias", "s_wada", "s_wqkv", "s_wp", "s_rowb", "s_w1", "s_w2"))
        s_xin, s_xres, s_gmsa, s_gmlp, s_gscr, s_qkscr, s_stack, s_mrow, s_mscr, s_zscr, s_out = (
            sem(n) for n in ("s_xin", "s_xres", "s_gmsa", "s_gmlp", "s_gscr", "s_qkscr", "s_stack", "s_mrow", "s_mscr", "s_zscr", "s_out"))
        t_set, a_set, v_set, p_set = (sem(n) for n in ("t_set", "a_set", "v_set", "p_set"))
        t_h1, t_qk, t_v, t_smax, t_m, t_st, t_pv, t_ot, t_ot2, t_proj, t_h2, t_f1, t_f2 = (
            sem(n) for n in ("t_h1", "t_qk", "t_v", "t_smax", "t_m", "t_st", "t_pv", "t_ot", "t_ot2",
                             "t_proj", "t_h2", "t_f1", "t_f2"))
        a_h1, a_qk, a_v, a_m, a_exp, a_oraw, a_oT, a_h2, a_gelu = (
            sem(n) for n in ("a_h1", "a_qk", "a_v", "a_m", "a_exp", "a_oraw", "a_oT", "a_h2", "a_gelu"))
        v_bn1, v_mv1, v_h1, v_qk, v_m, v_max, v_oraw, v_rec, v_otok, v_oT = (
            sem(n) for n in ("v_bn1", "v_mv1", "v_h1", "v_qk", "v_m", "v_max", "v_oraw",
                             "v_rec", "v_otok", "v_oT"))
        v_prod, v_x2, v_bn2, v_mv2, v_xn2, v_h2, v_ghi, v_y = (
            sem(n) for n in ("v_prod", "v_x2", "v_bn2", "v_mv2", "v_xn2", "v_h2", "v_ghi", "v_y"))
        p_ve1, p_rstd1, p_cent1, p_xn1, p_ve2, p_rstd2, p_xres, p_x2g, p_glo, p_y = (
            sem(n) for n in ("p_ve1", "p_rstd1", "p_cent1", "p_xn1", "p_ve2", "p_rstd2", "p_xres", "p_x2g", "p_glo", "p_y"))

        DX = 16
        N_STACK = 7 * DX
        N_SCR = 4 * DX
        x_b = x.rearrange("b (t p) c -> b p t c", p=P)
        out_b = out.rearrange("b (t p) c -> b p t c", p=P)

        HEAD_START = {
            "sp": [(s_out, DX)],
            "pe": [(t_ot, 1), (t_ot2, 1), (t_proj, 1), (t_h2, 1), (t_f1, NF1), (t_f2, NT)],
            "act": [(a_gelu, FT)],
            "dve": [(v_ghi, NF1), (v_y, NT), (v_x2, 1)],
            "pool": [(p_x2g, 1), (p_glo, NF1), (p_y, NT)],
        }

        def head_start(name, engine):
            for s, n in HEAD_START[name]:
                engine.sem_inc(s, n)

        block = ctx.enter_context(nc.Block())

        def first(b):
            return isinstance(b, int) and b == 0

        def batches(engine, step):
            step(0, 0, 2)
            step(1, 1, 2)
            with engine.Fori(1, (B - 2) // 2) as pair:
                step(pair * 2, 0, 2)
                step(pair * 2 + 1, 1, 2)
            step(B - 2, 0, 1)
            step(B - 1, 1, 0)

        @block.sync
        def _(sp):
            head_start("sp", sp)

            def of(dram, b):
                return dram[b] if isinstance(b, int) else dram[bass.ds(b, 1)].rearrange("a p t c -> (a p) t c")

            def load_x(b):
                if not (isinstance(b, int) and b == 0):
                    sp.wait_ge(p_xn1, b)
                sp.dma_start(x_in[:, :, :], of(x_b, b)).then_inc(s_xin, DX)

            def load_gates(b, n, s_g):
                gate_b = gate_scr[bass.ds(b, 1), :] if not isinstance(b, int) else gate_scr[b:b + 1, :]
                sp.dma_start(gates[:, 2 * n:2 * n + 2, :].rearrange("p s c -> p (s c)"),
                             gate_b[:, 2 * C * n:2 * C * (n + 1)].broadcast_to([P, 2 * C])).then_inc(s_g, DX)

            def store(b):
                sp.wait_ge(p_y, b * NT + (NT + NT))
                sp.dma_start(of(out_b, b), result[:, :, :]).then_inc(s_out, DX)

            def stack(b, par):
                if isinstance(b, int) and b == 0:
                    sp.wait_ge(p_set, done(POOL_STEPS, "k_stack0"))
                    sp.wait_ge(s_zscr, 2 * DX)
                elif isinstance(b, int) and b == 1:
                    sp.wait_ge(p_set, done(POOL_STEPS, "k_stack1"))
                if not (isinstance(b, int) and b == 0):
                    sp.wait_ge(s_stack, b * N_STACK)
                sp.wait_ge(a_qk, b * 4 + 4)
                sp.wait_ge(v_qk, b * 4 + 4)
                for n, t in enumerate((qk_hi, qk_lo)):
                    for m in range(2):
                        sp.dma_start(qk_scr[2 * m + n].rearrange("(k p) t -> p k t", p=P),
                                     t[:, KC * m:KC * (m + 1), :].bitcast(F32)).then_inc(s_qkscr, DX)
                if not (isinstance(b, int) and b < 2):
                    sp.wait_ge(t_st, (b - 1) * NCH)
                sp.dma_start(q_stack[par][ZROW:ZROW + 2, :, :].bitcast(F32), max_scr[1]).then_inc(s_stack, DX)
                sp.wait_ge(s_qkscr, b * N_SCR + N_SCR)
                for dst, pieces in ((q_stack[par], (0, 1, 0)), (k_stack[par], (2, 2, 3))):
                    for r, piece in enumerate(pieces):
                        sp.dma_start(dst[D * r:D * (r + 1), :, :].bitcast(F32),
                                     qk_scr[piece].rearrange("(h d) t -> d h t", d=D)).then_inc(s_stack, DX)

            def max_rows(b, par):
                sp.wait_ge(a_m, b + 1)
                sp.wait_ge(v_m, b + 1)
                for r, t in enumerate((m_hi, m_lo)):
                    sp.dma_start(max_scr[0, r], t[:, :].bitcast(F32)).then_inc(s_mscr, DX)
                sp.wait_ge(s_mscr, b * 2 * DX + 2 * DX)
                sp.dma_start(q_stack[par][ZROW:ZROW + 2, :, :].bitcast(F32), max_scr[0]).then_inc(s_mrow, DX)

            sp.dma_start(cond_sb, cond).then_inc(s_cond, DX)
            for r0, v in ((R_ADA, b_ada), (R_QKV, b_qkv), (R_B1, b1)):
                n = v.shape[0] // P
                sp.dma_start(bias_rows[r0:r0 + n, :], v.rearrange("(r p) -> r p", p=P)).then_inc(s_bias, DX)
            load_x(0)
            sp.dma_start(wada_raw, w_ada.rearrange("(k p) n -> p k n", p=P)).then_inc(s_wada, DX)
            sp.dma_start(wqkv_raw, w_qkv.rearrange("(k p) n -> p k n", p=P)).then_inc(s_wqkv, DX)
            sp.dma_start(wp_raw, w_proj.rearrange("(k p) n -> p k n", p=P)).then_inc(s_wp, DX)
            for n, v in enumerate((b_ada[2 * C:3 * C], b_ada[5 * C:6 * C], b_proj, b2)):
                sp.dma_start(row_bias[:, n, :], v.rearrange("(a c) -> a c", a=1).broadcast_to([B, C])
                             ).then_inc(s_rowb, DX)
            sp.wait_ge(p_set, done(POOL_STEPS, "zero_rows"))
            for r in range(2):
                sp.dma_start(max_scr[1, r], zero_rows[:, :]).then_inc(s_zscr, DX)
            load_x(1)
            stack(0, 0)
            sp.wait_ge(t_set, done(TENSOR_STEPS, "gate_rows"))
            sp.dma_start(w1_raw, w1.rearrange("(k p) n -> p k n", p=P)).then_inc(s_w1, DX)
            stack(1, 1)
            sp.wait_ge(a_set, done(SCALAR_STEPS, "wqkv_hi"))
            sp.wait_ge(v_set, done(VECTOR_STEPS, "wqkv_lo"))
            sp.dma_start(w2_raw, w2.rearrange("(k p) n -> p k n", p=P)).then_inc(s_w2, DX)
            sp.wait_ge(v_set, done(VECTOR_STEPS, "gate_mlp_bias"))
            sp.dma_start(gate_scr, rows.rearrange("b s c -> b (s c)")).then_inc(s_gscr, DX)
            sp.wait_ge(s_gscr, DX)
            max_rows(0, 0)

            def step(b, par, ahead):
                if ahead == 2:
                    load_x(b + 2)
                sp.wait_ge(v_x2, b + 1)
                load_gates(b, 0, s_gmsa)
                sp.dma_start(x_res[:, :, :], of(x_b, b)).then_inc(s_xres, DX)
                if ahead == 2:
                    stack(b + 2, par)
                if ahead >= 1:
                    max_rows(b + 1, 1 - par)
                if not first(b):
                    store(b - 1)
                load_gates(b, 1, s_gmlp)

            batches(sp, step)
            store(B - 1)
            sp.wait_ge(s_out, B * DX + DX)

        @block.tensor
        def _(pe):
            head_start("pe", pe)

            def three(out_ap, a_hi, a_lo, b_hi, b_lo, first, last):
                pe.matmul(out_ap, a_hi, b_hi, start=first, stop=False)
                pe.matmul(out_ap, a_hi, b_lo, start=False, stop=False)
                return pe.matmul(out_ap, a_lo, b_hi, start=False, stop=last)

            def norm_T(b):
                pe.wait_ge(p_xn1, b + 1)
                for k in range(KC):
                    for t in range(NT):
                        last = pe.transpose(ps[:, k, P * t:P * (t + 1)],
                                            xn[:, t, P * k:P * (k + 1)], ident[:, :])
                last.then_inc(t_h1, 1)

            def qk_tiles(b, m, bank):
                pe.wait_ge(a_h1, b * KC + KC)
                pe.wait_ge(v_h1, b * KC + KC)
                for j in range(KC):
                    c = C * m + P * j
                    for k in range(KC):
                        last = three(halves(bank)[:, j, :], wqkv_hi[:, k, c:c + P], wqkv_lo[:, k, c:c + P],
                                     h1_hi[:, k, :], h1_lo[:, k, :], k == 0, k == KC - 1)
                last.then_inc(t_qk, 1)

            def v_tiles(b):
                for t in range(NT):
                    for k in range(KC):
                        tt = slice(P * t, P * (t + 1))
                        last = three(halves(2)[:, t, :], h1_hi[:, k, tt], h1_lo[:, k, tt],
                                     wqkv_hi[:, k, 2 * C:3 * C], wqkv_lo[:, k, 2 * C:3 * C],
                                     k == 0, k == KC - 1)
                last.then_inc(t_v, 1)

            def max_scores(b, par, s):
                t, hp = s // (H // 2), s % (H // 2)
                if s == 0:
                    pe.wait_ge(s_stack, b * N_STACK + N_STACK)
                if s >= 2:
                    pe.wait_ge(v_max, b * NMX + (s - 1))
                for u in range(2):
                    h = 2 * hp + u
                    last = pe.matmul(halves(4 + s % 2)[:, u, :], q_stack[par][:, h, P * t:P * (t + 1)],
                                     k_stack[par][:, h, :], start=True, stop=True)
                last.then_inc(t_smax, 1)

            def max_T(b):
                pe.wait_ge(v_max, b * NMX + NMX)
                for t in range(NT):
                    last = pe.transpose(ps[0:H, 5, P * t:P * (t + 1)], neg_max[:, t, :], ident[:, :])
                last.then_inc(t_m, 1)

            def scores(b, par, c):
                g, t = c // NT, c % NT
                if c >= 2:
                    pe.wait_ge(a_exp, b * NCH + (c - 1))
                for u in range(HG):
                    h = HG * g + u
                    last = pe.matmul(halves(2 * (c % 2) + u // 2)[:, u % 2, :],
                                     k_stack[par][:, h, P * t:P * (t + 1)], q_stack[par][:, h, :],
                                     start=True, stop=True)
                last.then_inc(t_st, 1)

            def p_v(b, par, c):
                g, t = c // NT, c % NT
                pe.wait_ge(a_exp, b * NCH + (c + 1))
                for u in range(HG):
                    last = pe.matmul(halves(6 + g // 2)[32 * u:32 * (u + 1), g % 2, :],
                                     v_ext[par][:, t, HG * g + u, :],
                                     probs[:, c % 4, T * u:T * (u + 1)],
                                     start=(t == 0), stop=(t == NT - 1))
                last.then_inc(t_pv, 1)

            def mlp_out(b, between=lambda: None):
                for f in range(FT):
                    if f == FT - 2:
                        between()
                    if f % 2 == 0:
                        pe.wait_ge(v_ghi, b * NF1 + (NF1 + f // 2 + 1))
                        pe.wait_ge(p_glo, b * NF1 + (NF1 + f // 2 + 1))
                    for t in range(NT):
                        tt = slice(P * t, P * (t + 1))
                        last = three(ps[:, (6, 0)[t], 0:C], g_hi[:, f, tt], g_lo[:, f, tt],
                                     w2_hi[:, f, :], w2_lo[:, f, :], f == 0, f == FT - 1)
                        if f == FT - 1:
                            last.then_inc(t_f2, 1)

            pe.wait_ge(p_set, done(POOL_STEPS, "ident"))
            pe.wait_ge(s_cond, DX)
            for k in range(KC):
                last = pe.transpose(ps[:, 7, B * k:B * (k + 1)], cond_sb[:, P * k:P * (k + 1)], ident[0:B, 0:B])
            last.then_inc(t_set, 1)
            pe.wait_ge(s_bias, 3 * DX)
            pe.transpose(ps[:, 6, 0:NROW], bias_rows, ident[0:NROW, 0:NROW]).then_inc(t_set, 1)
            pe.wait_ge(v_set, done(VECTOR_STEPS, "silu"))
            pe.wait_ge(s_wada, DX)
            for m in (*range(SHIFT1, SCALE1 + KC), *range(SHIFT2, SCALE2 + KC)):
                for k in range(KC):
                    last = pe.matmul(ps[:, 4, B * m:B * (m + 1)], wada_raw[:, k, P * m:P * (m + 1)],
                                     silu_T[:, k, :], start=(k == 0), stop=(k == KC - 1))
            last.then_inc(t_set, 1)
            norm_T(0)
            pe.wait_ge(v_set, done(VECTOR_STEPS, "mod_msa"))
            pe.wait_ge(s_wqkv, DX)
            for m in range(3 * KC):
                for k in range(KC):
                    last = pe.matmul(ps[:, 3, B * m:B * (m + 1)], wqkv_raw[:, k, P * m:P * (m + 1)],
                                     mod_T[:, SHIFT1 + k, :], start=(k == 0), stop=(k == KC - 1))
            last.then_inc(t_set, 1)
            pe.wait_ge(a_set, done(SCALAR_STEPS, "wqkv_hi"))
            pe.wait_ge(v_set, done(VECTOR_STEPS, "wqkv_lo"))
            qk_tiles(0, 0, 1)
            qk_tiles(0, 1, 0)
            v_tiles(0)
            for n, c in enumerate((2 * C, 5 * C)):
                for k in range(KC):
                    last = pe.matmul(ps[0:B, 5, C * n:C * (n + 1)], silu_T[:, k, :], wada_raw[:, k, c:c + C],
                                     start=(k == 0), stop=(k == KC - 1))
            last.then_inc(t_set, 1)
            pe.wait_ge(a_qk, 4)
            pe.wait_ge(v_qk, 4)
            norm_T(1)
            qk_tiles(1, 0, 1)
            qk_tiles(1, 1, 0)
            pe.wait_ge(a_v, 1)
            v_tiles(1)
            pe.wait_ge(v_set, done(VECTOR_STEPS, "qkv_bias"))
            pe.wait_ge(s_wp, DX)
            for k in range(KC):
                last = pe.matmul(ps[0:B, 6, 0:C], qkv_bias[:, 2 * KC + k, :], wp_raw[:, k, :],
                                 start=(k == 0), stop=(k == KC - 1))
            last.then_inc(t_set, 1)
            pe.wait_ge(v_set, done(VECTOR_STEPS, "gate_rows"))
            for s in range(NMX):
                max_scores(0, 0, s)
            max_T(0)
            pe.wait_ge(s_w1, DX)
            for m in range(FT):
                for k in range(KC):
                    last = pe.matmul(ps[:, 7, B * m:B * (m + 1)], w1_raw[:, k, P * m:P * (m + 1)],
                                     mod_T[:, SHIFT2 + k, :], start=(k == 0), stop=(k == KC - 1))
            last.then_inc(t_set, 1)
            pe.wait_ge(a_qk, 8)
            pe.wait_ge(v_qk, 8)
            pe.wait_ge(a_set, done(SCALAR_STEPS, "w1_hi"))
            pe.wait_ge(v_set, done(VECTOR_STEPS, "wp_lo"))
            pe.wait_ge(p_set, done(POOL_STEPS, "w1_lo"))
            pe.wait_ge(v_set, done(VECTOR_STEPS, "mlp_bias"))
            pe.wait_ge(a_m, 1)
            pe.wait_ge(v_m, 1)

            def step(b, par, ahead):
                if ahead:
                    pe.wait_ge(a_gelu, b * FT + 4)
                    max_scores(b + 1, 1 - par, 0)
                    max_scores(b + 1, 1 - par, 1)
                pe.wait_ge(a_v, b + 2 if ahead else b + 1)
                pe.wait_ge(s_mrow, b * DX + DX)
                pe.wait_ge(a_gelu, b * FT + FT)
                scores(b, par, 0)
                scores(b, par, 1)
                for c in range(NCH + 1):
                    if ahead and 0 < c < NCH:
                        max_scores(b + 1, 1 - par, 2 * c)
                        max_scores(b + 1, 1 - par, 2 * c + 1)
                    if c == NCH and ahead == 2:
                        norm_T(b + 2)
                    if c:
                        p_v(b, par, c - 1)
                    if c and c + 1 < NCH:
                        scores(b, par, c + 1)

                if ahead:
                    max_T(b + 1)
                pe.wait_ge(a_oraw, b + 1)
                pe.wait_ge(v_oraw, b + 1)
                for t in range(NT):
                    for g in range(H // HG):
                        last = pe.transpose(ps[:, 2 + t, P * g:P * (g + 1)], o_raw[:, g, P * t:P * (t + 1)],
                                            ident[:, :])
                last.then_inc(t_ot, 1)
                if ahead == 2:
                    qk_tiles(b + 2, 0, 1)
                pe.wait_ge(v_otok, b + 1)
                for k in range(KC):
                    for t in range(NT):
                        last = pe.transpose(halves(6)[:, k, P * t:P * (t + 1)], o_tok[:, t, P * k:P * (k + 1)],
                                            ident[:, :])
                last.then_inc(t_ot2, 1)
                if ahead == 2:
                    qk_tiles(b + 2, 1, 0)
                pe.wait_ge(a_oT, b + 1)
                pe.wait_ge(v_oT, b + 1)
                for t in range(NT):
                    for k in range(KC):
                        tt = slice(P * t, P * (t + 1))
                        last = three(halves(7)[:, t, :], oT_hi[:, k, tt], oT_lo[:, k, tt],
                                     wp_hi[:, k, :], wp_lo[:, k, :], k == 0, k == KC - 1)
                last.then_inc(t_proj, 1)
                if ahead == 2:
                    v_tiles(b + 2)

                def norm2_T():
                    if ahead == 2:
                        pe.wait_ge(a_v, b + 3)
                    pe.wait_ge(v_xn2, b * NT + NT)
                    for k in range(KC):
                        for t in range(NT):
                            last = pe.transpose(ps[:, 3 - k, P * t:P * (t + 1)],
                                                xn[:, t, P * k:P * (k + 1)], ident[:, :])
                    last.then_inc(t_h2, 1)

                if first(b):
                    norm2_T()
                    pe.wait_ge(a_set, done(SCALAR_STEPS, "w2_hi"))
                    pe.wait_ge(p_set, done(POOL_STEPS, "w2_lo"))
                else:
                    if ahead == 2:
                        pe.wait_ge(a_qk, b * 4 + 12)
                        pe.wait_ge(v_qk, b * 4 + 12)
                    mlp_out(b - 1, norm2_T)
                if ahead == 2:
                    pe.wait_ge(a_qk, b * 4 + 12)
                    pe.wait_ge(v_qk, b * 4 + 12)
                if ahead:
                    pe.wait_ge(a_m, b + 2)
                    pe.wait_ge(v_m, b + 2)
                pe.wait_ge(a_h2, b * KC + KC)
                pe.wait_ge(v_h2, b * KC + KC)
                for f in range(FT):
                    if f == 4:
                        pe.wait_ge(v_y, b * NT + NT)
                    for k in range(KC):
                        ff = slice(P * f, P * (f + 1))
                        last = three(halves((4, 5, 0, 1)[f // 2])[:, f % 2, :], w1_hi[:, k, ff],
                                     w1_lo[:, k, ff], h2_hi[:, k, :], h2_lo[:, k, :], k == 0, k == KC - 1)
                    if f % 2:
                        last.then_inc(t_f1, 1)

            batches(pe, step)
            pe.wait_ge(a_gelu, B * FT + 6)
            mlp_out(B - 1)

        @block.scalar
        def _(act):
            head_start("act", act)

            def of(b):
                return bass.ds(b, 1) if not isinstance(b, int) else slice(b, b + 1)

            def h1_part(b):
                act.wait_ge(t_h1, b + 1)
                if not (isinstance(b, int) and b == 0):
                    act.wait_ge(t_v, b)
                for k in range(KC):
                    act.activation(h1_hi[:, k, :], ps[:, k, 0:T], ACT.Copy,
                                   scale=mod_T[:, SCALE1 + k, of(b)]).then_inc(a_h1, 1)

            def qk_part(b, m):
                if m == 0 and not (isinstance(b, int) and b == 0):
                    act.wait_ge(s_qkscr, b * N_SCR)
                act.wait_ge(t_qk, b * 2 + (m + 1))
                for j in range(KC):
                    act.activation(qk_hi[:, KC * m + j, :], halves(1 - m)[:, j, :], ACT.Identity,
                                   bias=qkv_bias[:, KC * m + j, of(b)]).then_inc(a_qk, 1)

            def v_part(b, par):
                act.wait_ge(t_v, b + 1)
                act.activation(v_ext[par][:, :, :, 0:D],
                               halves(2).rearrange("p t (h d) -> p t h d", d=D), ACT.Copy).then_inc(a_v, 1)

            def m_part(b):
                act.wait_ge(t_m, b + 1)
                if not (isinstance(b, int) and b == 0):
                    act.wait_ge(s_mscr, b * 2 * DX)
                act.activation(m_hi[:, :], ps[0:H, 5, 0:T], ACT.Copy).then_inc(a_m, 1)

            act.wait_ge(t_set, done(TENSOR_STEPS, "cond_T"))
            act.activation(exp_c[:, :, :], ps[:, 7, 0:KC * B].rearrange("p (k b) -> p k b", k=KC), ACT.Exp,
                           scale=-1.0).then_inc(a_set, 1)
            act.wait_ge(s_wqkv, DX)
            act.activation(wqkv_hi[:, :, :], wqkv_raw, ACT.Copy).then_inc(a_set, 1)
            act.wait_ge(v_set, done(VECTOR_STEPS, "scale_msa"))
            h1_part(0)
            act.wait_ge(v_set, done(VECTOR_STEPS, "qkv_bias"))
            qk_part(0, 0)
            qk_part(0, 1)
            act.wait_ge(p_set, done(POOL_STEPS, "v_one1"))
            v_part(0, 0)
            h1_part(1)
            qk_part(1, 0)
            qk_part(1, 1)
            v_part(1, 1)
            act.wait_ge(s_wp, DX)
            act.activation(wp_hi[:, :, :], wp_raw, ACT.Copy).then_inc(a_set, 1)
            act.wait_ge(s_w1, DX)
            act.activation(w1_hi[:, :, :], w1_raw, ACT.Copy).then_inc(a_set, 1)
            m_part(0)
            act.wait_ge(s_w2, DX)
            act.activation(w2_hi[:, :, :], w2_raw, ACT.Copy).then_inc(a_set, 1)
            act.wait_ge(v_set, done(VECTOR_STEPS, "mlp_bias"))
            act.wait_ge(p_set, done(POOL_STEPS, "w1_lo"))
            act.wait_ge(t_set, done(TENSOR_STEPS, "mlp_bias"))

            def step(b, par, ahead):
                for c in range(NCH):
                    if c == NCH - 1:
                        act.wait_ge(t_pv, b * NCH + NCH // 2)
                        act.wait_ge(t_ot, b + 1)
                        act.activation(o_raw[:, 0:2, :], halves(6), ACT.Copy).then_inc(a_oraw, 1)
                    act.wait_ge(t_st, b * NCH + (c + 1))
                    if c >= 4:
                        act.wait_ge(t_pv, b * NCH + (c - 3))
                    act.activation(probs[:, c % 4, :], ps[:, 2 * (c % 2):2 * (c % 2) + 2, :]
                                   .rearrange("p a n -> p (a n)"), ACT.Exp, scale=SCALE).then_inc(a_exp, 1)
                if ahead == 2:
                    h1_part(b + 2)
                    qk_part(b + 2, 0)
                act.wait_ge(t_ot2, b + 2)
                act.wait_ge(t_proj, b + 1)
                act.activation(oT_hi[:, :, :], halves(6), ACT.Copy).then_inc(a_oT, 1)
                if ahead:
                    m_part(b + 1)
                if ahead == 2:
                    qk_part(b + 2, 1)
                    v_part(b + 2, par)
                act.wait_ge(t_h2, b + 2)
                act.wait_ge(t_f1, b * NF1 + NF1)
                for k in range(KC):
                    act.activation(h2_hi[:, k, :], ps[:, 3 - k, 0:T], ACT.Copy,
                                   scale=mod_T[:, SCALE2 + k, of(b)]).then_inc(a_h2, 1)
                if first(b):
                    act.wait_ge(p_set, done(POOL_STEPS, "w2_lo"))
                act.wait_ge(v_ghi, b * NF1 + NF1)
                act.wait_ge(p_glo, b * NF1 + NF1)
                for f in range(FT):
                    if f % 2 == 0:
                        act.wait_ge(t_f1, b * NF1 + (NF1 + f // 2 + 1))
                    act.activation(gelu[:, f, :], halves((4, 5, 0, 1)[f // 2])[:, f % 2, :],
                                   ACT.Gelu_apprx_tanh, bias=mlp_bias[:, f, of(b)]).then_inc(a_gelu, 1)

            batches(act, step)

        @block.vector
        def _(dve):
            head_start("dve", dve)

            def of(b):
                return bass.ds(b, 1) if not isinstance(b, int) else slice(b, b + 1)

            def norm_stats(src, b, stats, mv, s_bn, s_mv, between):
                for t in range(NT):
                    dve.bn_stats(stats[:, t, :], src[:, t, :]).then_inc(s_bn, 1)
                dve.wait_ge(s_bn, b * NT + NT)
                between()
                for t in range(NT):
                    dve.bn_aggr(mv[:, t, :], stats[:, t, :]).then_inc(s_mv, 1)

            def norm_apply(src, b, mv, rstd, dst, s_rstd, s_xn):
                dve.wait_ge(s_rstd, b + 1)
                for t in range(NT):
                    dve.tensor_scalar(dst[:, t, :], src[:, t, :], mv[:, t, 0:1], rstd[:, t:t + 1],
                                      ALU.subtract, ALU.mult).then_inc(s_xn, 1)

            def norm1_stats(b, between=lambda: None):
                dve.wait_ge(s_xin, b * DX + DX)
                norm_stats(x_in, b, stats1, mv1, v_bn1, v_mv1, between)

            def h1_part(b):
                if not (isinstance(b, int) and b == 0):
                    dve.wait_ge(t_v, b)
                for k in range(KC):
                    dve.wait_ge(a_h1, b * KC + (k + 1))
                    dve.scalar_tensor_tensor(h1_lo[:, k, :], ps[:, k, 0:T], mod_T[:, SCALE1 + k, of(b)],
                                             h1_hi[:, k, :].bitcast(F32), ALU.mult, ALU.subtract
                                             ).then_inc(v_h1, 1)

            def qk_part(b, m):
                if m == 0 and not (isinstance(b, int) and b == 0):
                    dve.wait_ge(s_qkscr, b * N_SCR)
                dve.wait_ge(a_qk, b * 4 + (KC * m + KC))
                for j in range(KC):
                    n = KC * m + j
                    dve.scalar_tensor_tensor(qk_lo[:, n, :], halves(1 - m)[:, j, :], qkv_bias[:, n, of(b)],
                                             qk_hi[:, n, :].bitcast(F32), ALU.add, ALU.subtract
                                             ).then_inc(v_qk, 1)

            def reduce_max(b, s):
                t, hp = s // (H // 2), s % (H // 2)
                if s == 0 and not (isinstance(b, int) and b == 0):
                    dve.wait_ge(t_m, b)
                dve.wait_ge(t_smax, b * NMX + (s + 1))
                dve.tensor_reduce(neg_max[:, t, 2 * hp:2 * hp + 2], halves(4 + s % 2), AX.X, ALU.max,
                                  negate=True).then_inc(v_max, 1)

            def m_part(b):
                dve.wait_ge(a_m, b + 1)
                if not (isinstance(b, int) and b == 0):
                    dve.wait_ge(s_mscr, b * 2 * DX)
                dve.tensor_tensor(m_lo[:, :], ps[0:H, 5, 0:T], m_hi[:, :].bitcast(F32), ALU.subtract
                                  ).then_inc(v_m, 1)

            def wide(ap2, n):
                return ap2.unsqueeze(2).broadcast_to([ap2.shape[0], ap2.shape[1], n])

            dve.wait_ge(a_set, done(SCALAR_STEPS, "exp_cond"))
            dve.tensor_scalar(exp_c[:, :, :], exp_c[:, :, :], 1.0, None, ALU.add).then_inc(v_set, 1)
            dve.wait_ge(v_set, done(VECTOR_STEPS, "plus_one"))
            dve.reciprocal(cond_T[:, :, :], exp_c[:, :, :]).then_inc(v_set, 1)
            dve.wait_ge(v_set, done(VECTOR_STEPS, "recip"))
            dve.tensor_tensor(silu_T[:, :, :], ps[:, 7, 0:KC * B].rearrange("p (k b) -> p k b", k=KC),
                              cond_T[:, :, :], ALU.mult).then_inc(v_set, 1)
            dve.wait_ge(t_set, done(TENSOR_STEPS, "bias_T"))
            dve.tensor_copy(bias_T[:, :], ps[:, 6, 0:NROW]).then_inc(v_set, 1)
            norm1_stats(0)
            dve.wait_ge(v_set, done(VECTOR_STEPS, "bias_T"))
            dve.wait_ge(t_set, done(TENSOR_STEPS, "mod_T"))
            for m0 in (SHIFT1, SHIFT2):
                dve.tensor_tensor(mod_T[:, m0:m0 + 2 * KC, :],
                                  ps[:, 4, B * m0:B * (m0 + 2 * KC)].rearrange("p (m b) -> p m b", b=B),
                                  wide(bias_T[:, m0:m0 + 2 * KC], B), ALU.add).then_inc(v_set, 1)
            dve.wait_ge(v_set, done(VECTOR_STEPS, "mod_mlp"))
            for m0 in (SCALE1, SCALE2):
                dve.tensor_scalar(mod_T[:, m0:m0 + KC, :], mod_T[:, m0:m0 + KC, :], 1.0, None, ALU.add
                                  ).then_inc(v_set, 1)
            dve.wait_ge(a_set, done(SCALAR_STEPS, "wqkv_hi"))
            dve.tensor_tensor(wqkv_lo[:, :, :], wqkv_raw, wqkv_hi[:, :, :].bitcast(F32), ALU.subtract
                              ).then_inc(v_set, 1)
            dve.wait_ge(v_set, done(VECTOR_STEPS, "scale_msa"))
            h1_part(0)
            dve.wait_ge(t_set, done(TENSOR_STEPS, "qkv_bias"))
            dve.tensor_tensor(qkv_bias[:, :, :], ps[:, 3, 0:3 * KC * B].rearrange("p (m b) -> p m b", b=B),
                              wide(bias_T[:, R_QKV:R_QKV + 3 * KC], B), ALU.add).then_inc(v_set, 1)
            norm1_stats(1)
            dve.wait_ge(v_set, done(VECTOR_STEPS, "qkv_bias"))
            qk_part(0, 0)
            qk_part(0, 1)
            h1_part(1)
            qk_part(1, 0)
            qk_part(1, 1)
            dve.wait_ge(s_rowb, 4 * DX)
            dve.wait_ge(t_set, done(TENSOR_STEPS, "gate_rows"))
            dve.tensor_tensor(rows[:, 0:3:2, :], halves(5)[0:B], row_bias[:, 0:2, :], ALU.add
                              ).then_inc(v_set, 1)
            dve.wait_ge(t_set, done(TENSOR_STEPS, "proj_bias"))
            dve.tensor_tensor(rows[:, 1, :], ps[0:B, 6, 0:C], row_bias[:, 2, :], ALU.add
                              ).then_inc(v_set, 1)
            dve.wait_ge(v_set, done(VECTOR_STEPS, "proj_bias"))
            dve.tensor_tensor(rows[:, 1, :], rows[:, 1, :], rows[:, 0, :], ALU.mult).then_inc(v_set, 1)
            dve.tensor_tensor(rows[:, 3, :], row_bias[:, 3, :], rows[:, 2, :], ALU.mult).then_inc(v_set, 1)
            dve.wait_ge(a_set, done(SCALAR_STEPS, "wp_hi"))
            dve.tensor_tensor(wp_lo[:, :, :], wp_raw, wp_hi[:, :, :].bitcast(F32), ALU.subtract
                              ).then_inc(v_set, 1)
            for s in range(NMX):
                reduce_max(0, s)
            m_part(0)
            dve.wait_ge(t_set, done(TENSOR_STEPS, "mlp_bias"))
            dve.tensor_tensor(mlp_bias[:, :, :], ps[:, 7, 0:FT * B].rearrange("p (m b) -> p m b", b=B),
                              wide(bias_T[:, R_B1:R_B1 + FT], B), ALU.add).then_inc(v_set, 1)
            dve.wait_ge(s_gscr, DX)

            def gate(n):
                return gates[:, n:n + 1, :].broadcast_to([P, NT, C])

            def mlp_gate(b):
                dve.wait_ge(s_gmlp, b * DX + DX)
                dve.wait_ge(s_out, b * DX + DX)
                for t in range(NT):
                    dve.wait_ge(t_f2, b * NT + (NT + t + 1))
                    dve.tensor_tensor(result[:, t, :], ps[:, (6, 0)[t], 0:C], gates[:, 2, :], ALU.mult
                                      ).then_inc(v_y, 1)

            def step(b, par, ahead):
                if ahead:
                    for s in range(0 if first(b) else 2, NMX):
                        if ahead == 2 and s == NMX // 2:
                            norm1_stats(b + 2, lambda: reduce_max(b + 1, s))
                        else:
                            reduce_max(b + 1, s)
                dve.wait_ge(t_pv, b * NCH + NCH)
                dve.wait_ge(t_ot, b + 1)
                dve.tensor_copy(o_raw[:, 2:4, :], halves(7)).then_inc(v_oraw, 1)
                if ahead == 2:
                    h1_part(b + 2)
                dve.wait_ge(t_ot, b + 2)
                o_ps = ps[:, 2:4, :].rearrange("p t (h e) -> p (t h) e", e=32)
                dve.reciprocal(den_rec[:, :], o_ps[:, :, D]).then_inc(v_rec, 1)
                dve.wait_ge(v_rec, b + 1)
                dve.wait_ge(t_ot2, b + 1)
                dve.tensor_tensor(o_tok[:, :, :].rearrange("p t (h d) -> p (t h) d", d=D), o_ps[:, :, 0:D],
                                  wide(den_rec[:, :], D), ALU.mult).then_inc(v_otok, 1)
                dve.wait_ge(a_oT, b + 1)
                dve.wait_ge(t_proj, b + 1)
                dve.tensor_tensor(oT_lo[:, :, :], halves(6), oT_hi[:, :, :].bitcast(F32), ALU.subtract
                                  ).then_inc(v_oT, 1)
                if ahead == 2:
                    qk_part(b + 2, 0)
                    qk_part(b + 2, 1)
                dve.wait_ge(t_proj, b + 2)
                dve.wait_ge(s_gmsa, b * DX + DX)
                dve.wait_ge(p_x2g, b + 1)
                dve.tensor_tensor(x2[:, :, :], halves(7), gate(0), ALU.mult).then_inc(v_prod, 1)
                dve.wait_ge(v_prod, b + 1)
                dve.wait_ge(p_xres, b + 1)
                dve.tensor_tensor(x2[:, :, :], x2[:, :, :], x_res[:, :, :], ALU.add).then_inc(v_x2, 1)
                dve.wait_ge(v_x2, b + 2)
                norm_stats(x2, b, stats2, mv2, v_bn2, v_mv2, (lambda: m_part(b + 1)) if ahead else lambda: None)
                dve.wait_ge(t_h2, b + 1)
                norm_apply(x2, b, mv2, rstd2, xn, p_rstd2, v_xn2)
                for k in range(KC):
                    dve.wait_ge(a_h2, b * KC + (k + 1))
                    dve.scalar_tensor_tensor(h2_lo[:, k, :], ps[:, 3 - k, 0:T], mod_T[:, SCALE2 + k, of(b)],
                                             h2_hi[:, k, :].bitcast(F32), ALU.mult, ALU.subtract
                                             ).then_inc(v_h2, 1)
                if not first(b):
                    mlp_gate(b - 1)
                dve.wait_ge(t_f2, b * NT + NT)
                for j in range(NF1):
                    dve.wait_ge(a_gelu, b * FT + (FT + 2 * j + 2))
                    dve.tensor_copy(g_hi[:, 2 * j:2 * j + 2, :], gelu[:, 2 * j:2 * j + 2, :]).then_inc(v_ghi, 1)
                    if ahead == 2 and j == 1:
                        reduce_max(b + 2, 0)
                        reduce_max(b + 2, 1)

            batches(dve, step)
            mlp_gate(B - 1)

        @block.gpsimd
        def _(pool):
            head_start("pool", pool)

            def rstd_of(b, mv, ve, rstd, s_mv, s_ve, s_rstd):
                pool.wait_ge(s_mv, b * NT + NT)
                pool.tensor_tensor(ve[:, :], mv[:, :, 1], eps[:, :], ALU.add).then_inc(s_ve, 1)
                pool.wait_ge(s_ve, b + 1)
                pool.tensor_tensor(rstd[:, :], ve[:, :], minus_half[:, :], ALU.pow).then_inc(s_rstd, 1)

            def final_sum(b):
                pool.wait_ge(p_x2g, b + 2)
                for t in range(NT):
                    pool.wait_ge(v_y, b * NT + (NT + t + 1))
                    pool.tensor_tensor(result[:, t, :], result[:, t, :], x2g[:, t, :], ALU.add).then_inc(p_y, 1)

            def rstd1_of(b):
                rstd_of(b, mv1, ve1, rstd1, v_mv1, p_ve1, p_rstd1)

            def norm1_apply(b):
                if not (isinstance(b, int) and b == 0):
                    pool.wait_ge(t_h1, b)
                pool.wait_ge(p_rstd1, b + 1)
                pool.tensor_tensor(xn[:, :, :], x_in[:, :, :], mv1[:, :, 0:1].broadcast_to([P, NT, C]),
                                   ALU.subtract).then_inc(p_cent1, 1)
                pool.wait_ge(p_cent1, b + 1)
                pool.tensor_tensor(xn[:, :, :], xn[:, :, :], rstd1[:, :].unsqueeze(2).broadcast_to([P, NT, C]),
                                   ALU.mult).then_inc(p_xn1, 1)

            pool.memset(minus_half[:, :], -0.5).then_inc(p_set, 1)
            pool.memset(eps[:, :], EPS).then_inc(p_set, 1)
            pool.memset(ident[:, :], 0.0).then_inc(p_set, 1)
            pool.wait_ge(p_set, done(POOL_STEPS, "ident_zero"))
            pool.affine_select(out=ident[:, :], in_=ident[:, :], compare_op=ALU.not_equal, fill=1.0, base=0,
                               pattern=[[-1, P]], channel_multiplier=1).then_inc(p_set, 1)
            pool.memset(zero_rows[:, :], 0.0).then_inc(p_set, 1)
            rstd1_of(0)
            norm1_apply(0)
            for i in range(2):
                pool.memset(v_ext[i][:, :, :, D:32], 0.0).then_inc(p_set, 1)
            pool.wait_ge(p_set, done(POOL_STEPS, "v_zero1"))
            for i in range(2):
                pool.memset(v_ext[i][:, :, :, D:D + 1], 1.0).then_inc(p_set, 1)
            for i in range(2):
                pool.memset(q_stack[i][:, :, :].bitcast(F32), 0.0).then_inc(p_set, 1)
                pool.memset(k_stack[i][:, :, :].bitcast(F32), 1.0).then_inc(p_set, 1)
            rstd1_of(1)
            norm1_apply(1)
            pool.wait_ge(a_set, done(SCALAR_STEPS, "w1_hi"))
            pool.tensor_tensor(w1_lo[:, :, :], w1_raw, w1_hi[:, :, :].bitcast(F32), ALU.subtract
                               ).then_inc(p_set, 1)
            pool.wait_ge(a_set, done(SCALAR_STEPS, "w2_hi"))
            pool.tensor_tensor(w2_lo[:, :, :], w2_raw, w2_hi[:, :, :].bitcast(F32), ALU.subtract
                               ).then_inc(p_set, 1)

            def step(b, par, ahead):
                pool.wait_ge(s_gmsa, b * DX + DX)
                pool.wait_ge(s_xres, b * DX + DX)
                pool.tensor_tensor(x_res[:, :, :], x_res[:, :, :], gates[:, 1:2, :].broadcast_to([P, NT, C]),
                                   ALU.add).then_inc(p_xres, 1)
                if ahead == 2:
                    rstd1_of(b + 2)
                    pool.wait_ge(t_h2, b + 1)
                    norm1_apply(b + 2)
                rstd_of(b, mv2, ve2, rstd2, v_mv2, p_ve2, p_rstd2)
                if not first(b):
                    final_sum(b - 1)
                pool.wait_ge(p_y, b * NT + NT)
                pool.wait_ge(s_gmlp, b * DX + DX)
                pool.tensor_tensor(x2g[:, :, :], x2[:, :, :], gates[:, 3:4, :].broadcast_to([P, NT, C]),
                                   ALU.add).then_inc(p_x2g, 1)
                for j in range(NF1):
                    jj = slice(2 * j, 2 * j + 2)
                    pool.wait_ge(v_ghi, b * NF1 + (NF1 + j + 1))
                    if j == 0:
                        pool.wait_ge(t_f2, b * NT + NT)
                    pool.tensor_tensor(g_lo[:, jj, :], gelu[:, jj, :], g_hi[:, jj, :].bitcast(F32),
                                       ALU.subtract).then_inc(p_glo, 1)

            batches(pool, step)
            final_sum(B - 1)


_INS = ['x', 'cond_1024', 'L0_cond_w_qkv', 'L0_cond_b_qkv', 'L0_cond_w_proj', 'L0_cond_b_proj',
        'L0_cond_w_ada', 'L0_cond_b_ada', 'L0_cond_w1', 'L0_cond_b1', 'L0_cond_w2', 'L0_cond_b2']


def kernel(**inputs):
    import numpy as _np
    import concourse.bacc as _bacc
    from concourse import mybir as _mybir
    from concourse.bass_utils import run_bass_kernel_spmd as _run

    nc = _bacc.Bacc("TRN2", target_bir_lowering=False, num_devices=1)
    arrays, args = {}, []
    for name in _INS:
        a = _np.ascontiguousarray(inputs[name])
        arrays[f"in_{name}_dram"] = a
        args.append(nc.dram_tensor(f"in_{name}_dram", a.shape, _mybir.dt.from_np(a.dtype), kind="ExternalInput").ap())
    shape = inputs['x'].shape
    args.append(nc.dram_tensor("out_0_dram", shape, _mybir.dt.from_np(_np.dtype('float32')), kind="ExternalOutput").ap())
    adaln_block_kernel(nc, *args)
    r = _run(nc, [arrays], core_ids=[0])
    return r.results[0]["out_0_dram"]
```
